# Optimizing a Trainium2 kernel written in Bass

```python
import numpy as np
import jax
import jax.numpy as jnp

def _softmax(x, axis=-1):
    return jax.nn.softmax(x, axis=axis)

def _gelu(x):
    return jax.nn.gelu(x, approximate=True)

def _silu(x):
    return jax.nn.silu(x)

def _sigmoid(x):
    return jax.nn.sigmoid(x)

def _layernorm(x, axis=-1, eps=1e-05):
    m = jnp.mean(x, axis=axis, keepdims=True)
    v = jnp.var(x, axis=axis, keepdims=True)
    return (x - m) / jnp.sqrt(v + eps)

def _scatter_add(tgt, idx, src, axis=0):
    return tgt.at[idx].add(src)

def _segment_sum(src, seg, n):
    return jax.ops.segment_sum(src, seg, n)
kernel_name = 'mk_dlrm_tower_d1_rec_r8_3a6094'

def setup_inputs(seed: int=0):
    np.random.seed(seed)
    _w = jnp.asarray

    def _rec_inputs():
        import jax
        import jax.numpy as jnp
        _tk = jax.random.key(seed)
        ids = jnp.stack([jax.random.randint(jax.random.fold_in(_tk, 200 + f), (512,), 0, v, jnp.int32) for f, v in enumerate([1000, 125000, 12500, 12500, 1000, 12500, 1250, 1000, 1000, 1250, 1000, 1250, 1250, 12500, 12500, 12500, 1000, 1250, 1000, 1000, 1250, 1250, 1000, 1250, 1000, 1000])], axis=1)
        tbl_0 = 0.05 * jax.random.normal(jax.random.fold_in(_tk, 500 + 0), (1000, 128), jnp.float32)
        tbl_1 = 0.05 * jax.random.normal(jax.random.fold_in(_tk, 500 + 1), (125000, 128), jnp.float32)
        tbl_2 = 0.05 * jax.random.normal(jax.random.fold_in(_tk, 500 + 2), (12500, 128), jnp.float32)
        tbl_3 = 0.05 * jax.random.normal(jax.random.fold_in(_tk, 500 + 3), (12500, 128), jnp.float32)
        tbl_4 = 0.05 * jax.random.normal(jax.random.fold_in(_tk, 500 + 4), (1000, 128), jnp.float32)
        tbl_5 = 0.05 * jax.random.normal(jax.random.fold_in(_tk, 500 + 5), (12500, 128), jnp.float32)
        tbl_6 = 0.05 * jax.random.normal(jax.random.fold_in(_tk, 500 + 6), (1250, 128), jnp.float32)
        tbl_7 = 0.05 * jax.random.normal(jax.random.fold_in(_tk, 500 + 7), (1000, 128), jnp.float32)
        tbl_8 = 0.05 * jax.random.normal(jax.random.fold_in(_tk, 500 + 8), (1000, 128), jnp.float32)
        tbl_9 = 0.05 * jax.random.normal(jax.random.fold_in(_tk, 500 + 9), (1250, 128), jnp.float32)
        tbl_10 = 0.05 * jax.random.normal(jax.random.fold_in(_tk, 500 + 10), (1000, 128), jnp.float32)
        tbl_11 = 0.05 * jax.random.normal(jax.random.fold_in(_tk, 500 + 11), (1250, 128), jnp.float32)
        tbl_12 = 0.05 * jax.random.normal(jax.random.fold_in(_tk, 500 + 12), (1250, 128), jnp.float32)
        tbl_13 = 0.05 * jax.random.normal(jax.random.fold_in(_tk, 500 + 13), (12500, 128), jnp.float32)
        tbl_14 = 0.05 * jax.random.normal(jax.random.fold_in(_tk, 500 + 14), (12500, 128), jnp.float32)
        tbl_15 = 0.05 * jax.random.normal(jax.random.fold_in(_tk, 500 + 15), (12500, 128), jnp.float32)
        tbl_16 = 0.05 * jax.random.normal(jax.random.fold_in(_tk, 500 + 16), (1000, 128), jnp.float32)
        tbl_17 = 0.05 * jax.random.normal(jax.random.fold_in(_tk, 500 + 17), (1250, 128), jnp.float32)
        tbl_18 = 0.05 * jax.random.normal(jax.random.fold_in(_tk, 500 + 18), (1000, 128), jnp.float32)
        tbl_19 = 0.05 * jax.random.normal(jax.random.fold_in(_tk, 500 + 19), (1000, 128), jnp.float32)
        tbl_20 = 0.05 * jax.random.normal(jax.random.fold_in(_tk, 500 + 20), (1250, 128), jnp.float32)
        tbl_21 = 0.05 * jax.random.normal(jax.random.fold_in(_tk, 500 + 21), (1250, 128), jnp.float32)
        tbl_22 = 0.05 * jax.random.normal(jax.random.fold_in(_tk, 500 + 22), (1000, 128), jnp.float32)
        tbl_23 = 0.05 * jax.random.normal(jax.random.fold_in(_tk, 500 + 23), (1250, 128), jnp.float32)
        tbl_24 = 0.05 * jax.random.normal(jax.random.fold_in(_tk, 500 + 24), (1000, 128), jnp.float32)
        tbl_25 = 0.05 * jax.random.normal(jax.random.fold_in(_tk, 500 + 25), (1000, 128), jnp.float32)
        _rk = jax.random.fold_in(_tk, 7)
        r_dense_features = -0.000520686 + 1.00062 * jax.random.normal(jax.random.fold_in(_rk, 101), (512, 128), jnp.float32)
        W_top1 = 0.0405887 * jax.random.normal(jax.random.fold_in(_tk, 801), (607, 512), jnp.float32)
        W_top2 = 0.0441942 * jax.random.normal(jax.random.fold_in(_tk, 802), (512, 256), jnp.float32)
        W_top3 = 0.0625 * jax.random.normal(jax.random.fold_in(_tk, 803), (256, 1), jnp.float32)
        b_top1 = jnp.zeros((512,), jnp.float32)
        b_top2 = jnp.zeros((256,), jnp.float32)
        return (r_dense_features, ids, tbl_0, tbl_1, tbl_2, tbl_3, tbl_4, tbl_5, tbl_6, tbl_7, tbl_8, tbl_9, tbl_10, tbl_11, tbl_12, tbl_13, tbl_14, tbl_15, tbl_16, tbl_17, tbl_18, tbl_19, tbl_20, tbl_21, tbl_22, tbl_23, tbl_24, tbl_25, W_top1, b_top1, W_top2, b_top2, W_top3)
    r_dense_features, ids, tbl_0, tbl_1, tbl_2, tbl_3, tbl_4, tbl_5, tbl_6, tbl_7, tbl_8, tbl_9, tbl_10, tbl_11, tbl_12, tbl_13, tbl_14, tbl_15, tbl_16, tbl_17, tbl_18, tbl_19, tbl_20, tbl_21, tbl_22, tbl_23, tbl_24, tbl_25, W_top1, b_top1, W_top2, b_top2, W_top3 = _rec_inputs()

    def _L0_rec_setup():
        import jax, jax.numpy as jnp
        import numpy as np
        B, F, D = (2048, 26, 128)
        key = jax.random.key(seed)
        k1, k2 = jax.random.split(key)
        dense_features = jax.random.normal(k1, (B, D), dtype=jnp.float32)
        sparse_values = jax.random.normal(k2, (B, F, D), dtype=jnp.float32)
        return {'dense_features': dense_features, 'sparse_values': sparse_values}
    _L0_rec_all = _L0_rec_setup()
    _L0_rec_in = {k: v for k, v in _L0_rec_all.items() if k in ()}
    del _L0_rec_all
    return {'r_dense_features': r_dense_features, 'ids': ids, 'tbl_0': tbl_0, 'tbl_1': tbl_1, 'tbl_2': tbl_2, 'tbl_3': tbl_3, 'tbl_4': tbl_4, 'tbl_5': tbl_5, 'tbl_6': tbl_6, 'tbl_7': tbl_7, 'tbl_8': tbl_8, 'tbl_9': tbl_9, 'tbl_10': tbl_10, 'tbl_11': tbl_11, 'tbl_12': tbl_12, 'tbl_13': tbl_13, 'tbl_14': tbl_14, 'tbl_15': tbl_15, 'tbl_16': tbl_16, 'tbl_17': tbl_17, 'tbl_18': tbl_18, 'tbl_19': tbl_19, 'tbl_20': tbl_20, 'tbl_21': tbl_21, 'tbl_22': tbl_22, 'tbl_23': tbl_23, 'tbl_24': tbl_24, 'tbl_25': tbl_25, 'W_top1': W_top1, 'b_top1': b_top1, 'W_top2': W_top2, 'b_top2': b_top2, 'W_top3': W_top3}

def reference(r_dense_features, ids, tbl_0, tbl_1, tbl_2, tbl_3, tbl_4, tbl_5, tbl_6, tbl_7, tbl_8, tbl_9, tbl_10, tbl_11, tbl_12, tbl_13, tbl_14, tbl_15, tbl_16, tbl_17, tbl_18, tbl_19, tbl_20, tbl_21, tbl_22, tbl_23, tbl_24, tbl_25, W_top1, b_top1, W_top2, b_top2, W_top3):
    import jax
    import jax.numpy as jnp

    def _L0_rec_ref(dense_features, sparse_values):
        import jax, jax.numpy as jnp
        import numpy as np
        B, F, D = (2048, 26, 128)
        sd = jnp.einsum('bfd,bd->bf', sparse_values, dense_features)
        ss = jnp.einsum('bfd,bgd->bfg', sparse_values, sparse_values)
        iu, ju = jnp.triu_indices(F, k=1)
        pairs = ss[:, iu, ju]
        return jnp.concatenate([dense_features, sd, pairs], axis=1)
    e = jnp.stack([tbl_0[ids[:, 0]], tbl_1[ids[:, 1]], tbl_2[ids[:, 2]], tbl_3[ids[:, 3]], tbl_4[ids[:, 4]], tbl_5[ids[:, 5]], tbl_6[ids[:, 6]], tbl_7[ids[:, 7]], tbl_8[ids[:, 8]], tbl_9[ids[:, 9]], tbl_10[ids[:, 10]], tbl_11[ids[:, 11]], tbl_12[ids[:, 12]], tbl_13[ids[:, 13]], tbl_14[ids[:, 14]], tbl_15[ids[:, 15]], tbl_16[ids[:, 16]], tbl_17[ids[:, 17]], tbl_18[ids[:, 18]], tbl_19[ids[:, 19]], tbl_20[ids[:, 20]], tbl_21[ids[:, 21]], tbl_22[ids[:, 22]], tbl_23[ids[:, 23]], tbl_24[ids[:, 24]], tbl_25[ids[:, 25]]], axis=1)
    z = _L0_rec_ref(r_dense_features, e)
    z = z.reshape(z.shape[0], -1)
    h = jnp.concatenate([z, r_dense_features], axis=1)
    h = jnp.maximum(h @ W_top1 + b_top1, 0.0)
    h = jnp.maximum(h @ W_top2 + b_top2, 0.0)
    y = h @ W_top3
    return y

_drawn_inputs = setup_inputs


def setup_inputs(seed=0):
    import zlib

    import numpy as np

    out = dict(_drawn_inputs(seed))
    spreads = {'b_top1': (0.0, 0.1), 'b_top2': (0.0, 0.1)}
    factors = {}
    for name, (base, spread) in spreads.items():
        noise = np.random.default_rng([zlib.crc32(name.encode()), seed]).standard_normal(out[name].shape)
        drawn = base * np.exp(spread * noise) if base else spread * noise
        out[name] = jnp.asarray(drawn.astype(out[name].dtype))
    for name, factor in factors.items():
        out[name] = (out[name] * factor).astype(out[name].dtype)
    return out
```

```python
import concourse.bass as bass
from concourse import mybir
from contextlib import ExitStack

B, F, D = 512, 26, 128
P = 128
TILES = B // P
H1, H2 = 512, 256
VOCAB = 1000
MATCHED = [0, 4, 7, 8, 16, 18, 19, 22, 24]
GATHERED = [f for f in range(F) if f not in MATCHED]
NM, NG = len(MATCHED), len(GATHERED)
NV = F + 1
SLOT_VECTORS = [0] + [1 + f for f in MATCHED] + [1 + f for f in GATHERED]
G0 = 1 + NM
SLOTS = 32
ROWS = 8
TP = VOCAB // ROWS
MASKS = 8
CA = 13
NA1, NA2 = NV - 1, NV - 1 - CA
PAIRS1 = CA * NA1
PAIRS = PAIRS1 + (NV - 1 - CA) * NA2
KC = 4
KP = -(-PAIRS // KC)
GJ = 8
GROUPS = [list(range(NG))[i:i + 4] for i in range(0, NG, 4)]
C_BATCHES = [(0, 8), (8, 13), (13, 21), (21, 26)]


def pair_rows():
    out = []
    for c in range(NV - 1):
        for a in range(c + 1, NV):
            n = c * NA1 + a - 1 if c < CA else PAIRS1 + (c - CA) * NA2 + a - CA - 1
            u, v = sorted((SLOT_VECTORS[c], SLOT_VECTORS[a]))
            row = D + v - 1 if u == 0 else D + F + (u - 1) * F - u * (u - 1) // 2 + v - u - 1
            out.append((n // KP, n % KP, row))
    return out


def program(nc, dense, ids, ids_row, tables, w1p, w1, b1, w2, b2, w3, out):
    fp32, f32r, i32 = mybir.dt.float32, mybir.dt.float32r, mybir.dt.int32
    ALU, ACT = mybir.AluOpType, mybir.ActivationFunctionType
    ctx = ExitStack()
    with ctx:
        def sb(name, shape, dt=fp32):
            return ctx.enter_context(nc.sbuf_tensor(name, shape, dt))

        def ps(name, shape):
            return ctx.enter_context(nc.psum_tensor(name, shape, fp32))

        def sem(name):
            return ctx.enter_context(nc.semaphore(name))

        ident = sb("ident", [P, P])
        row_no = sb("row_no", [TP, ROWS])
        idx = sb("idx", [P, TILES, F], i32)
        idsb = sb("idsb", [TP, NM, B], i32)
        raw = sb("raw", [TP, 2, ROWS * D])
        hi = [sb(f"hi{i}", [TP, ROWS * D], f32r) for i in range(2)]
        lo = [sb(f"lo{i}", [TP, ROWS * D], f32r) for i in range(2)]
        mask = [sb(f"mask{i}", [TP, B], f32r) for i in range(MASKS)]
        rows = sb("rows", [P, TILES, NG, D])
        dense_sb = sb("dense_sb", [P, TILES, D])
        embT = sb("embT", [P, B, SLOTS])
        denseT = sb("denseT", [P, TILES, 4, P // 4])
        gram = sb("gram", [P, NV - 1, P // 4])
        pairs = sb("pairs", [P, KC * KP])
        pairsT = sb("pairsT", [KP, KC, P])
        w1_sb = sb("w1_sb", [P, KC, H1])
        w1a = sb("w1a", [P, H1])
        w1b = sb("w1b", [P, H1])
        w1d = sb("w1d", [P, H1])
        w2_sb = sb("w2_sb", [P, H1 // P, H2])
        w3_sb = sb("w3_sb", [P, H2 // P])
        b1_sb = sb("b1_sb", [P, H1 // P])
        b2_sb = sb("b2_sb", [P, H2 // P])
        h1 = sb("h1", [P, H1 // P, P])
        h2 = sb("h2", [P, H2 // P, P])
        y = sb("y", [1, B])

        bank = ps("bank", [P, 2, 512])
        wide = ps("wide", [P, 2, GJ, P])
        h1_ps = ps("h1_ps", [P, H1 // P, P])
        h2_ps = ps("h2_ps", [P, 4, P])

        ids_in = sem("ids_in")
        idsb_in = [sem(f"idsb_in{m}") for m in range(NM)]
        raw_in = [sem("raw_in0"), sem("raw_in1")]
        dense_in = sem("dense_in")
        w1_in = sem("w1_in")
        w_in = sem("w_in")
        rows_in = [[sem(f"rows_in{t}_{g}") for g in range(len(GROUPS))] for t in range(TILES)]
        ident_zero = sem("ident_zero")
        ident_ready = sem("ident_ready")
        row_no_ready = sem("row_no_ready")
        spare_ready = sem("spare_ready")
        w1d_ready = sem("w1d_ready")
        hi_ready = sem("hi_ready")
        lo_ready = sem("lo_ready")
        mask_ready = sem("mask_ready")
        mask_used = sem("mask_used")
        bank_full = sem("bank_full")
        bank_moved = [sem("bank_moved0"), sem("bank_moved1")]
        wide_full = sem("wide_full")
        wide_moved = [sem("wide_moved0"), sem("wide_moved1")]
        h1_full = sem("h1_full")
        h1_moved = sem("h1_moved")
        h2_full = sem("h2_full")
        h2_moved = sem("h2_moved")
        y_full = sem("y_full")
        y_moved = sem("y_moved")
        out_done = sem("out_done")

        steps = [("dense", 0, 0)] + [("match", m, 0) for m in range(NM)]
        back = [[("turn", 0)], [("turn", 1)], [("turn", 2), ("turn", 3)], [("pairsT", 0), ("layer1", 0)],
                [("layer2", 0), ("layer3", 0)]]
        for t in range(TILES):
            for g in range(len(GROUPS)):
                steps.append(("fields", t, g))
                if t:
                    steps += [(kind, t - 1, k) for kind, k in back[g]] if g < len(back) else []
            if t:
                for part in back[len(GROUPS):]:
                    steps += [(kind, t - 1, k) for kind, k in part]
            steps += [("gram", t, k) for k in range(P // 4 // GJ)]
        for part in back:
            steps += [(kind, TILES - 1, k) for kind, k in part]
        BANK = ("dense", "match", "fields", "pairsT")
        WIDE = ("gram", "turn")
        bank_steps = [s for s in steps if s[0] in BANK]
        wide_steps = [s for s in steps if s[0] in WIDE]

        def bank_no(step):
            return bank_steps.index(step)

        def wide_no(step):
            return wide_steps.index(step)

        def wait_bank_moved(eng, n):
            eng.wait_ge(bank_moved[n % 2], n // 2 + 1)

        def wait_wide_moved(eng, n):
            eng.wait_ge(wide_moved[n % 2], 2 * (n // 2 + 1))

        def wait_bank_full(eng, step):
            if step[0] == "match":
                eng.wait_ge(mask_used, ROWS * (step[1] + 1))
            else:
                eng.wait_ge(bank_full, [s for s in bank_steps if s[0] != "match"].index(step) + 1)

        def fields_move(t, g):
            group = GROUPS[g]
            n = bank_no(("fields", t, g)) % 2
            dst = embT[:, t * P:(t + 1) * P, G0 + group[0]:G0 + group[0] + len(group)].rearrange("p b f -> p f b")
            return dst, bank[:, n, 0:len(group) * P].rearrange("p (f b) -> p f b", b=P)

        def gram_moves(t, k):
            n = wide_no(("gram", t, k)) % 2
            out = []
            for s in range(4):
                q = slice(SLOTS * s, SLOTS * (s + 1))
                src = wide[q, n, :, 0:4 * (NV - 1)].rearrange("p j (s c) -> p c j s", s=4)[:, :, :, s]
                out.append((gram[q, :, k * GJ:(k + 1) * GJ], src))
            return out

        def turn_moves(t, k):
            n = wide_no(("turn", t, k)) % 2
            c0, c1 = C_BATCHES[k]
            a0, na, at = (1, NA1, c0 * NA1) if c0 < CA else (CA + 1, NA2, PAIRS1 + (c0 - CA) * NA2)
            out = []
            for s in range(4):
                dst = pairs[32 * s:32 * (s + 1), at:at + (c1 - c0) * na].rearrange("p (c a) -> p c a", a=na)
                out.append((dst, wide[0:32, n, 0:c1 - c0, SLOTS * s + a0:SLOTS * s + NV]))
            return out

        block = ctx.enter_context(nc.Block())

        @block.sync
        def _(sp):
            sp.dma_start(idx[:, :, :], ids.rearrange("(t p) f -> p t f", p=P)).then_inc(ids_in, 16)
            for m, f in enumerate(MATCHED):
                if m >= 2:
                    sp.wait_ge(hi_ready, m - 1)
                    sp.wait_ge(lo_ready, m - 1)
                table = tables[f].rearrange("(p r) d -> p (r d)", r=ROWS)
                full = TP // 16 * 16
                sp.dma_start(raw[0:full, m % 2, :], table[0:full, :]).then_inc(raw_in[m % 2], 16)
                sp.dma_start(raw[full:TP, m % 2, :], table[full:TP, :]).then_inc(raw_in[m % 2], 16)
                if m == 0:
                    sp.dma_start(dense_sb[:, :, :], dense.rearrange("(t p) d -> p t d", p=P)).then_inc(dense_in, 16)
            sp.dma_start(w1_sb[:, :, :], w1p.rearrange("p (k n) -> p k n", k=KC)).then_inc(w_in, 16)
            sp.dma_start(w1a[:, :], w1[0:D, :]).then_inc(w1_in, 16)
            sp.dma_start(w1b[:, :], w1[D + F + F * (F - 1) // 2:, :]).then_inc(w1_in, 16)
            sp.dma_start(w2_sb[:, :, :], w2.rearrange("(k p) n -> p k n", p=P)).then_inc(w_in, 16)
            with nc.allow_non_contiguous_dma(reason="small vectors laid on partitions"):
                sp.dma_start(w3_sb[:, :], w3.rearrange("(k p) o -> p (k o)", p=P)).then_inc(w_in, 16)
                sp.dma_start(b1_sb[:, :], b1.rearrange("(k p) -> p k", p=P)).then_inc(w_in, 16)
                sp.dma_start(b2_sb[:, :], b2.rearrange("(k p) -> p k", p=P)).then_inc(w_in, 16)
            sp.wait_ge(y_moved, TILES)
            sp.dma_start(out.rearrange("b o -> o b"), y[:, :]).then_inc(out_done, 16)
            sp.wait_ge(out_done, 16)

        @block.gpsimd
        def _(pool):
            nc.gpsimd.iota(row_no[:, :], pattern=[[1, ROWS]], base=0, channel_multiplier=ROWS,
                           allow_small_or_imprecise_dtypes=True).then_inc(row_no_ready, 1)
            nc.gpsimd.memset(ident[:, :], 0.0).then_inc(ident_zero, 1)
            pool.wait_ge(ident_zero, 1)
            nc.gpsimd.affine_select(out=ident[:, :], in_=ident[:, :], compare_op=ALU.not_equal, fill=1.0, base=0,
                                    pattern=[[-1, P]], channel_multiplier=1).then_inc(ident_ready, 1)
            pool.wait_ge(ids_in, 16)
            for t in range(TILES):
                for g, group in enumerate(GROUPS):
                    for n in group:
                        f = GATHERED[n]
                        pool.indirect_dma_start(
                            out=rows[:, t, n, :], out_offset=None, in_=tables[f],
                            in_offset=bass.IndirectOffsetOnAxis(ap=idx[:, t, f:f + 1], axis=0),
                        ).then_inc(rows_in[t][g], 16)

        @block.scalar
        def _(act):
            for m, f in enumerate(MATCHED):
                act.dma_start(idsb[:, m, :], ids_row[m:m + 1, :].to_broadcast([TP, B])).then_inc(idsb_in[m], 16)

            def split(m):
                act.wait_ge(raw_in[m % 2], 32 * (m // 2 + 1))
                if m >= 2:
                    act.wait_ge(mask_used, ROWS * (m - 1))
                nc.scalar.activation(hi[m % 2][:, :], raw[:, m % 2, :], ACT.Copy).then_inc(hi_ready, 1)

            def move_bank(step, dst, src):
                n = bank_no(step)
                wait_bank_full(act, step)
                nc.scalar.activation(dst, src, ACT.Copy).then_inc(bank_moved[n % 2], 1)

            def move_wide(step, pieces, share=1):
                n = wide_no(step)
                act.wait_ge(wide_full, n + 1)
                for dst, src in pieces:
                    last = nc.scalar.activation(dst, src, ACT.Copy)
                last.then_inc(wide_moved[n % 2], share)

            split(0)
            for kind, t, k in steps:
                step = (kind, t, k)
                if kind == "dense":
                    src = bank[:, bank_no(step) % 2, :]
                    wait_bank_full(act, step)
                    nc.scalar.activation(denseT[:, :, :, :], src.rearrange("p (t j s) -> p t s j", s=4, t=TILES),
                                         ACT.Copy)
                    move_bank(step, embT[:, :, 0], src)
                elif kind == "match":
                    if t + 1 < NM:
                        split(t + 1)
                    move_bank(step, embT[:, :, 1 + t], bank[:, bank_no(step) % 2, :])
                elif kind == "fields" and bank_no(step) % 2 == 0:
                    dst, src = fields_move(t, k)
                    move_bank(step, dst, src)
                elif kind == "gram":
                    move_wide(step, gram_moves(t, k)[0:2])
                elif kind == "turn" and k % 2 == 0:
                    move_wide(step, turn_moves(t, k), 2)
                elif kind == "layer1":
                    act.wait_ge(h1_full, t + 1)
                    if t == 0:
                        act.wait_ge(w_in, 16 * 5)
                    for o in range(H1 // P):
                        last = nc.scalar.activation(h1[:, o, :], h1_ps[:, o, :], ACT.Relu, bias=b1_sb[:, o:o + 1])
                    last.then_inc(h1_moved, 1)

        @block.vector
        def _(dve):
            def masks(m):
                dve.wait_ge(idsb_in[m], 16)
                for r in range(ROWS):
                    n = m * ROWS + r
                    if n >= MASKS:
                        dve.wait_ge(mask_used, n - MASKS + 1)
                    nc.vector.tensor_scalar(mask[n % MASKS][:, :], idsb[:, m, :], row_no[:, r:r + 1], None,
                                            ALU.is_equal).then_inc(mask_ready, 1)

            def split(m):
                dve.wait_ge(hi_ready, m + 1)
                if m >= 2:
                    dve.wait_ge(mask_used, ROWS * (m - 1))
                nc.vector.tensor_tensor(lo[m % 2][:, :], raw[:, m % 2, :], hi[m % 2][:, :].bitcast(fp32),
                                        ALU.subtract).then_inc(lo_ready, 1)

            def move_bank(step, dst, src):
                n = bank_no(step)
                wait_bank_full(dve, step)
                nc.vector.tensor_copy(dst, src).then_inc(bank_moved[n % 2], 1)

            def move_wide(step, pieces, share=1):
                n = wide_no(step)
                dve.wait_ge(wide_full, n + 1)
                for dst, src in pieces:
                    last = nc.vector.tensor_copy(dst, src)
                last.then_inc(wide_moved[n % 2], share)

            nc.vector.memset(embT[:, :, NV:SLOTS], 0.0).then_inc(spare_ready, 1)
            if KC * KP > PAIRS:
                nc.vector.memset(pairs[:, PAIRS:KC * KP], 0.0).then_inc(spare_ready, 1)
            dve.wait_ge(row_no_ready, 1)
            for kind, t, k in steps:
                step = (kind, t, k)
                if kind == "match":
                    split(t)
                    masks(t)
                elif kind == "fields":
                    if t == 0 and k == 0:
                        dve.wait_ge(w1_in, 32)
                        nc.vector.tensor_tensor(w1d[:, :], w1a[:, :], w1b[:, :], ALU.add).then_inc(w1d_ready, 1)
                    if bank_no(step) % 2 == 1:
                        dst, src = fields_move(t, k)
                        move_bank(step, dst, src)
                elif kind == "gram":
                    move_wide(step, gram_moves(t, k)[2:4])
                elif kind == "turn" and k % 2 == 1:
                    move_wide(step, turn_moves(t, k), 2)
                elif kind == "pairsT":
                    move_bank(step, pairsT[:, :, :],
                              bank[0:KP, bank_no(step) % 2, :].rearrange("p (k b) -> p k b", b=P))
                elif kind == "layer2":
                    dve.wait_ge(h2_full, t + 1)
                    if t == 0:
                        dve.wait_ge(w_in, 16 * 5)
                    for o in range(H2 // P):
                        last = nc.vector.tensor_scalar(h2[:, o, :], h2_ps[:, o, :], b2_sb[:, o:o + 1], 0.0, ALU.add,
                                                       ALU.max)
                    last.then_inc(h2_moved, 1)
                elif kind == "layer3":
                    dve.wait_ge(y_full, t + 1)
                    nc.vector.tensor_copy(y[:, t * P:(t + 1) * P].rearrange("o (j s) -> o s j", s=4),
                                          h2_ps[0:1, 2, :].rearrange("o (s j) -> o s j", s=4)).then_inc(y_moved, 1)

        @block.tensor
        def _(pe):
            def bank_turn(step):
                n = bank_no(step)
                if n >= 2:
                    wait_bank_moved(pe, n - 2)
                return n % 2

            def wide_turn(step):
                n = wide_no(step)
                if n >= 2:
                    wait_wide_moved(pe, n - 2)
                return n % 2

            for kind, t, k in steps:
                step = (kind, t, k)
                if kind == "dense":
                    pe.wait_ge(ident_ready, 1)
                    pe.wait_ge(dense_in, 16)
                    n = bank_turn(step)
                    for i in range(TILES):
                        last = nc.tensor.transpose(bank[:, n, i * P:(i + 1) * P], dense_sb[:, i, :], ident[:, :])
                    last.then_inc(bank_full, 1)
                elif kind == "match":
                    n = bank_turn(step)
                    pe.wait_ge(lo_ready, t + 1)
                    for r in range(ROWS):
                        pe.wait_ge(mask_ready, t * ROWS + r + 1)
                        m = mask[(t * ROWS + r) % MASKS][:, :]
                        nc.tensor.matmul(bank[:, n, :], hi[t % 2][:, r * D:(r + 1) * D], m,
                                         start=(r == 0), stop=False)
                        last = nc.tensor.matmul(bank[:, n, :], lo[t % 2][:, r * D:(r + 1) * D], m,
                                                start=False, stop=(r == ROWS - 1))
                        last.then_inc(mask_used, 1)
                elif kind == "fields":
                    pe.wait_ge(rows_in[t][k], 16 * len(GROUPS[k]))
                    n = bank_turn(step)
                    for i, g in enumerate(GROUPS[k]):
                        last = nc.tensor.transpose(bank[:, n, i * P:(i + 1) * P], rows[:, t, g, :], ident[:, :])
                    last.then_inc(bank_full, 1)
                elif kind == "gram":
                    if k == 0:
                        u = bank_no(("fields", t, len(GROUPS) - 1))
                        wait_bank_moved(pe, u)
                        wait_bank_moved(pe, u - 1)
                        if t == 0:
                            pe.wait_ge(spare_ready, 1)
                    n = wide_turn(step)
                    for j in range(GJ):
                        b = t * P + 4 * (k * GJ + j)
                        last = nc.tensor.matmul(wide[:, n, j, 0:4 * (NV - 1)],
                                                embT[:, b:b + 4, :].rearrange("p s a -> p (s a)"),
                                                embT[:, b:b + 4, 0:NV - 1], start=True, stop=True)
                    last.then_inc(wide_full, 1)
                elif kind == "turn":
                    if k == 0:
                        u = wide_no(("gram", t, P // 4 // GJ - 1))
                        wait_wide_moved(pe, u)
                        wait_wide_moved(pe, u - 1)
                    n = wide_turn(step)
                    c0, c1 = C_BATCHES[k]
                    for c in range(c0, c1):
                        last = nc.tensor.transpose(wide[0:32, n, c - c0, :], gram[:, c, :], ident[:, :])
                    last.then_inc(wide_full, 1)
                elif kind == "pairsT":
                    u = wide_no(("turn", t, len(C_BATCHES) - 1))
                    wait_wide_moved(pe, u)
                    wait_wide_moved(pe, u - 1)
                    if t == 0:
                        pe.wait_ge(spare_ready, 2)
                    n = bank_turn(step)
                    for i in range(KC):
                        last = nc.tensor.transpose(bank[0:KP, n, i * P:(i + 1) * P], pairs[:, i * KP:(i + 1) * KP],
                                                   ident[:, :])
                    last.then_inc(bank_full, 1)
                elif kind == "layer1":
                    wait_bank_moved(pe, bank_no(("pairsT", t, 0)))
                    if t == 0:
                        pe.wait_ge(w_in, 16 * 5)
                        pe.wait_ge(w1d_ready, 1)
                    else:
                        pe.wait_ge(h1_moved, t)
                    x = denseT[:, t, :, :].rearrange("p s j -> p (s j)")
                    for o in range(H1 // P):
                        cols = slice(o * P, (o + 1) * P)
                        nc.tensor.matmul(h1_ps[:, o, :], w1d[:, cols], x, start=True, stop=False)
                        for i in range(KC):
                            last = nc.tensor.matmul(h1_ps[:, o, :], w1_sb[0:KP, i, cols], pairsT[:, i, :],
                                                    start=False, stop=(i == KC - 1))
                    last.then_inc(h1_full, 1)
                elif kind == "layer2":
                    pe.wait_ge(h1_moved, t + 1)
                    if t:
                        pe.wait_ge(y_moved, t)
                    for o in range(H2 // P):
                        for i in range(H1 // P):
                            last = nc.tensor.matmul(h2_ps[:, o, :], w2_sb[:, i, o * P:(o + 1) * P], h1[:, i, :],
                                                    start=(i == 0), stop=(i == H1 // P - 1))
                    last.then_inc(h2_full, 1)
                elif kind == "layer3":
                    pe.wait_ge(h2_moved, t + 1)
                    for i in range(H2 // P):
                        last = nc.tensor.matmul(h2_ps[0:1, 2, :], w3_sb[:, i:i + 1], h2[:, i, :],
                                                start=(i == 0), stop=(i == H2 // P - 1))
                    last.then_inc(y_full, 1)


def kernel(**inputs):
    import numpy as np
    import concourse.bacc as bacc
    from concourse import mybir
    from concourse.bass_utils import run_bass_kernel_spmd as run

    nc = bacc.Bacc("TRN2", target_bir_lowering=False, num_devices=1)
    data = {name: np.ascontiguousarray(a) for name, a in inputs.items()}
    data["ids_row"] = np.ascontiguousarray(data["ids"].T[MATCHED])
    w1p = np.zeros((P, KC, H1), data["W_top1"].dtype)
    chunk, part, row = (list(x) for x in zip(*pair_rows()))
    w1p[part, chunk] = data["W_top1"][row]
    data["w1p"] = w1p.reshape(P, KC * H1)
    arrays, h = {}, {}
    for name, a in data.items():
        arrays[name + "_in"] = a
        h[name] = nc.dram_tensor(name + "_in", a.shape, mybir.dt.from_np(a.dtype), kind="ExternalInput").ap()
    out = nc.dram_tensor("y_out", (B, 1), mybir.dt.float32, kind="ExternalOutput").ap()
    program(nc, h["r_dense_features"], h["ids"], h["ids_row"], [h[f"tbl_{f}"] for f in range(F)], h["w1p"],
            h["W_top1"], h["b_top1"], h["W_top2"], h["b_top2"], h["W_top3"], out)
    r = run(nc, [arrays], core_ids=[0])
    return r.results[0]["y_out"]
```

```python
import concourse.bass as bass
from concourse import mybir
from contextlib import ExitStack

B, F, D = 512, 26, 128
P = 128
TILES = B // P
H1, H2 = 512, 256
VOCAB = 1000
MATCHED = [0, 4, 7, 8, 16, 18, 19]
GATHERED = [f for f in range(F) if f not in MATCHED]
NM, NG = len(MATCHED), len(GATHERED)
NV = F + 1
SLOT_VECTORS = [0] + [1 + f for f in MATCHED] + [1 + f for f in GATHERED]
G0 = 1 + NM
SLOTS = 32
ROWS = 8
TP = VOCAB // ROWS
MASKS = 8
HALF = NV // 2
MERGED = HALF + 1
KC = -(-MERGED // 4)
KX = [len(range(x, MERGED, 4)) for x in range(4)]
KROWS = [SLOTS * min(4, MERGED - 4 * g) for g in range(KC)]
GROUPS = [list(range(NG))[i:i + 4] for i in range(0, NG, 4)]
NJ = P // 4
BATCHES = [[(j, j + n) for j in range(0, NJ, n)] for n in (8, 16, 16, 8)]


def serves_itself(k, a):
    return 1 <= a - k <= HALF


def pair_rows():
    out = []
    for k in range(MERGED):
        for a in range(NV):
            c = k if serves_itself(k, a) else k + HALF + 1
            if c < NV and c != a:
                u, v = sorted((SLOT_VECTORS[c], SLOT_VECTORS[a]))
                row = D + v - 1 if u == 0 else D + F + (u - 1) * F - u * (u - 1) // 2 + v - u - 1
                out.append((k // 4, SLOTS * (k % 4) + a, row))
    assert len({row for _, _, row in out}) == len(out) == NV * (NV - 1) // 2
    return out


def program(nc, dense, ids, ids_row, tables, w1p, w1, own_rows, b1, w2, b2, w3, out):
    fp32, f32r, i32 = mybir.dt.float32, mybir.dt.float32r, mybir.dt.int32
    ALU, ACT = mybir.AluOpType, mybir.ActivationFunctionType
    ctx = ExitStack()
    with ctx:
        def sb(name, shape, dt=fp32):
            return ctx.enter_context(nc.sbuf_tensor(name, shape, dt))

        def ps(name, shape):
            return ctx.enter_context(nc.psum_tensor(name, shape, fp32))

        def sem(name):
            return ctx.enter_context(nc.semaphore(name))

        ident = sb("ident", [P, P])
        row_no = sb("row_no", [TP, ROWS])
        idx = sb("idx", [P, TILES, F], i32)
        idsb = sb("idsb", [P, NM, B], i32)
        raw = sb("raw", [TP, 2, ROWS * D])
        hi = [sb(f"hi{i}", [TP, ROWS * D], f32r) for i in range(2)]
        lo = [sb(f"lo{i}", [TP, ROWS * D], f32r) for i in range(2)]
        mask = [sb(f"mask{i}", [TP, B], f32r) for i in range(MASKS)]
        rows = sb("rows", [P, TILES, NG, D])
        dense_sb = sb("dense_sb", [P, TILES, D])
        embT = sb("embT", [P, B, SLOTS])
        denseT = sb("denseT", [P, TILES, 4, P // 4])
        own = sb("own", [P, KC], i32)
        pairsT = [sb(f"pairsT{i}", [P, KC, 4, NJ]) for i in range(2)]
        w1_sb = sb("w1_sb", [P, KC, H1])
        w1a = sb("w1a", [P, H1])
        w1b = sb("w1b", [P, H1])
        w1d = sb("w1d", [P, H1])
        w2_sb = sb("w2_sb", [P, H1 // P, H2])
        w3_sb = sb("w3_sb", [P, H2 // P])
        b1_sb = sb("b1_sb", [P, H1 // P])
        b2_sb = sb("b2_sb", [P, H2 // P])
        h1 = sb("h1", [P, H1 // P, P])
        h2 = sb("h2", [P, H2 // P, P])
        y = sb("y", [1, B])

        bank = ps("bank", [P, 2, 512])
        wide = ps("wide", [P, 16, P])
        acc = [ps(f"acc{i}", [P, 4, P]) for i in range(2)]

        ids_in = sem("ids_in")
        idsb_in = [sem(f"idsb_in{m}") for m in range(NM)]
        raw_in = [sem("raw_in0"), sem("raw_in1")]
        dense_in = sem("dense_in")
        w1_in = sem("w1_in")
        w_in = sem("w_in")
        rows_in = [[sem(f"rows_in{t}_{g}") for g in range(len(GROUPS))] for t in range(TILES)]
        ident_zero = sem("ident_zero")
        ident_ready = sem("ident_ready")
        row_no_ready = sem("row_no_ready")
        spare_ready = sem("spare_ready")
        w1d_ready = sem("w1d_ready")
        hi_ready = sem("hi_ready")
        lo_ready = sem("lo_ready")
        mask_ready = sem("mask_ready")
        mask_used = sem("mask_used")
        bank_full = sem("bank_full")
        bank_moved = [sem("bank_moved0"), sem("bank_moved1")]
        wide_full = sem("wide_full")
        base_copied = sem("base_copied")
        wide_moved = sem("wide_moved")
        h1_full = sem("h1_full")
        h1_moved = [sem("h1_moved0"), sem("h1_moved1")]
        h2_full = sem("h2_full")
        h2_moved = [sem("h2_moved0"), sem("h2_moved1")]
        y_full = sem("y_full")
        y_moved = sem("y_moved")
        out_done = sem("out_done")

        LG, LT = len(GROUPS), TILES - 1
        fields = [("fields", t, g) for t in range(TILES) for g in range(LG)]
        early = iter(fields)
        steps = [("dense", 0, 0)]
        for m in range(NM):
            steps.append(("match", m, 0))
            steps += [next(early) for _ in range(0 if m < 1 else 1 if m < NM - 2 else 2)]

        def take(t, g):
            new = [f for f in fields if f <= ("fields", t, g) and f not in steps]
            steps.extend(new)

        for t in range(TILES):
            take(t, LG - 1)
            if t == LT:
                pass
            if t >= 2:
                steps.append(("layer3", t - 2, 0))
            for n in range(len(BATCHES[t])):
                steps.append(("gram", t, n))
                if n == 0 and 0 < t < LT:
                    steps.append(("layer1", t - 1, 0))
                elif n == 1 and 0 < t < LT:
                    steps.append(("layer2", t - 1, 0))
            if t == LT - 1:
                take(LT, 0)
                steps.append(("layer3", t - 1, 0))
                take(LT, 1)
                steps.append(("layer1", t, 0))
                take(LT, 2)
                steps.append(("layer2", t, 0))
                take(LT, 3)
                steps.append(("layer3", t, 0))
        steps = [x for n, x in enumerate(steps) if x not in steps[:n]]
        steps += [("layer1", LT, 0), ("layer2", LT, 0), ("layer3", LT, 0)]
        BANK = ("dense", "match", "fields")
        bank_steps = [s for s in steps if s[0] in BANK]
        wide_steps = [s for s in steps if s[0] == "gram"]

        def bank_no(step):
            return bank_steps.index(step)

        def wide_no(step):
            return wide_steps.index(step)

        def wait_bank_moved(eng, n):
            eng.wait_ge(bank_moved[n % 2], n // 2 + 1)

        def wait_bank_full(eng, step):
            if step[0] == "match":
                eng.wait_ge(mask_used, ROWS * (step[1] + 1))
            else:
                eng.wait_ge(bank_full, [s for s in bank_steps if s[0] != "match"].index(step) + 1)

        def fields_move(t, g):
            group = GROUPS[g]
            n = bank_no(("fields", t, g)) % 2
            dst = embT[:, t * P:(t + 1) * P, G0 + group[0]:G0 + group[0] + len(group)].rearrange("p b f -> p f b")
            return dst, bank[:, n, 0:len(group) * P].rearrange("p (f b) -> p f b", b=P)

        def merged(t, n, s, x, first):
            j0, j1 = BATCHES[t][n]
            at = j0 % 16
            dst = pairsT[t % 2][SLOTS * x:SLOTS * (x + 1), 0:KX[x], s, j0:j1]
            c = NV * s + first + x
            src = wide[SLOTS * s:SLOTS * (s + 1), at:at + j1 - j0, c:c + 4 * KX[x] - 3:4].rearrange("p j g -> p g j")
            return dst, src

        def moved_by_act(t, g):
            return t < 2 or bank_no(("fields", t, g)) % 2 == 0

        block = ctx.enter_context(nc.Block())

        @block.sync
        def _(sp):
            sp.dma_start(idx[:, :, :], ids.rearrange("(t p) f -> p t f", p=P)).then_inc(ids_in, 16)
            for m, f in enumerate(MATCHED):
                sp.dma_start(idsb[:, m, :], ids_row[m:m + 1, :].to_broadcast([P, B])).then_inc(idsb_in[m], 16)
                if m >= 2:
                    sp.wait_ge(hi_ready, m - 1)
                    sp.wait_ge(lo_ready, m - 1)
                table = tables[f].rearrange("(p r) d -> p (r d)", r=ROWS)
                full = TP // 16 * 16
                sp.dma_start(raw[0:full, m % 2, :], table[0:full, :]).then_inc(raw_in[m % 2], 16)
                sp.dma_start(raw[full:TP, m % 2, :], table[full:TP, :]).then_inc(raw_in[m % 2], 16)
                if m == 0:
                    sp.dma_start(dense_sb[:, :, :], dense.rearrange("(t p) d -> p t d", p=P)).then_inc(dense_in, 16)
            sp.dma_start(w1_sb[:, :, :], w1p.rearrange("p (k n) -> p k n", k=KC)).then_inc(w_in, 16)
            sp.dma_start(w1a[:, :], w1[0:D, :]).then_inc(w1_in, 16)
            sp.dma_start(w1b[:, :], w1[D + F + F * (F - 1) // 2:, :]).then_inc(w1_in, 16)
            sp.dma_start(w2_sb[:, :, :], w2.rearrange("(k p) n -> p k n", p=P)).then_inc(w_in, 16)
            with nc.allow_non_contiguous_dma(reason="small vectors laid on partitions"):
                sp.dma_start(own[:, :], own_rows).then_inc(w_in, 16)
                sp.dma_start(w3_sb[:, :], w3.rearrange("(k p) o -> p (k o)", p=P)).then_inc(w_in, 16)
                sp.dma_start(b1_sb[:, :], b1.rearrange("(k p) -> p k", p=P)).then_inc(w_in, 16)
                sp.dma_start(b2_sb[:, :], b2.rearrange("(k p) -> p k", p=P)).then_inc(w_in, 16)
            sp.wait_ge(y_moved, TILES)
            sp.dma_start(out.rearrange("b o -> o b"), y[:, :]).then_inc(out_done, 16)
            sp.wait_ge(out_done, 16)

        @block.gpsimd
        def _(pool):
            nc.gpsimd.iota(row_no[:, :], pattern=[[1, ROWS]], base=0, channel_multiplier=ROWS,
                           allow_small_or_imprecise_dtypes=True).then_inc(row_no_ready, 1)
            nc.gpsimd.memset(ident[:, :], 0.0).then_inc(ident_zero, 1)
            pool.wait_ge(ident_zero, 1)
            nc.gpsimd.affine_select(out=ident[:, :], in_=ident[:, :], compare_op=ALU.not_equal, fill=1.0, base=0,
                                    pattern=[[-1, P]], channel_multiplier=1).then_inc(ident_ready, 1)
            pool.wait_ge(ids_in, 16)
            for t in range(TILES):
                for g, group in enumerate(GROUPS):
                    for n in group:
                        f = GATHERED[n]
                        pool.indirect_dma_start(
                            out=rows[:, t, n, :], out_offset=None, in_=tables[f],
                            in_offset=bass.IndirectOffsetOnAxis(ap=idx[:, t, f:f + 1], axis=0),
                        ).then_inc(rows_in[t][g], 16)

        @block.scalar
        def _(act):
            def split(m):
                act.wait_ge(raw_in[m % 2], 32 * (m // 2 + 1))
                if m >= 2:
                    act.wait_ge(mask_used, ROWS * (m - 1))
                nc.scalar.activation(hi[m % 2][:, :], raw[:, m % 2, :], ACT.Copy).then_inc(hi_ready, 1)

            def move_bank(step, dst, src):
                n = bank_no(step)
                wait_bank_full(act, step)
                nc.scalar.activation(dst, src, ACT.Copy).then_inc(bank_moved[n % 2], 1)

            split(0)
            for kind, t, k in steps:
                step = (kind, t, k)
                if kind == "dense":
                    src = bank[:, bank_no(step) % 2, :]
                    wait_bank_full(act, step)
                    nc.scalar.activation(denseT[:, :, :, :], src.rearrange("p (t j s) -> p t s j", s=4, t=TILES),
                                         ACT.Copy)
                    move_bank(step, embT[:, :, 0], src)
                elif kind == "match":
                    if t + 1 < NM:
                        split(t + 1)
                    move_bank(step, embT[:, :, 1 + t], bank[:, bank_no(step) % 2, :])
                elif kind == "fields" and moved_by_act(t, k):
                    dst, src = fields_move(t, k)
                    move_bank(step, dst, src)
                elif kind == "gram":
                    act.wait_ge(wide_full, wide_no(step) + 1)
                    for s in range(4):
                        for x in range(4):
                            dst, src = merged(t, k, s, x, HALF + 1)
                            last = nc.scalar.activation(dst, src, ACT.Copy)
                        last.then_inc(base_copied, 1)
                elif kind == "layer1":
                    act.wait_ge(h1_full, 2 * t + 1)
                    if t == 0:
                        act.wait_ge(w_in, 16 * 6)
                    for o in range(2):
                        last = nc.scalar.activation(h1[:, o, :], acc[0][:, o, :], ACT.Relu, bias=b1_sb[:, o:o + 1])
                    last.then_inc(h1_moved[0], 1)
                elif kind == "layer2":
                    act.wait_ge(h2_full, 2 * t + 1)
                    nc.scalar.activation(h2[:, 0, :], acc[0][:, 2, :], ACT.Relu,
                                         bias=b2_sb[:, 0:1]).then_inc(h2_moved[0], 1)

        @block.vector
        def _(dve):
            def masks(m, chunks=range(ROWS)):
                dve.wait_ge(idsb_in[m], 16)
                for r in chunks:
                    n = m * ROWS + r
                    if n >= MASKS:
                        dve.wait_ge(mask_used, n - MASKS + 1)
                    nc.vector.tensor_scalar(mask[n % MASKS][:, :], idsb[0:TP, m, :], row_no[:, r:r + 1], None,
                                            ALU.is_equal).then_inc(mask_ready, 1)

            def split(m):
                dve.wait_ge(hi_ready, m + 1)
                if m >= 2:
                    dve.wait_ge(mask_used, ROWS * (m - 1))
                nc.vector.tensor_tensor(lo[m % 2][:, :], raw[:, m % 2, :], hi[m % 2][:, :].bitcast(fp32),
                                        ALU.subtract).then_inc(lo_ready, 1)

            def move_bank(step, dst, src):
                n = bank_no(step)
                wait_bank_full(dve, step)
                nc.vector.tensor_copy(dst, src).then_inc(bank_moved[n % 2], 1)

            nc.vector.memset(embT[:, :, NV:SLOTS], 0.0).then_inc(spare_ready, 1)
            nc.vector.memset(wide[:, :, 4 * NV:4 * NV + 1], 0.0).then_inc(spare_ready, 1)
            dve.wait_ge(row_no_ready, 1)
            for kind, t, k in steps:
                step = (kind, t, k)
                if kind == "match":
                    if t == 0:
                        masks(0)
                        split(0)
                    if t + 1 < NM:
                        masks(t + 1, range(0, 4))
                        split(t + 1)
                        masks(t + 1, range(4, ROWS))
                elif kind == "fields":
                    if t == 1 and k == LG - 1:
                        dve.wait_ge(w1_in, 32)
                        nc.vector.tensor_tensor(w1d[:, :], w1a[:, :], w1b[:, :], ALU.add).then_inc(w1d_ready, 1)
                    if not moved_by_act(t, k):
                        dst, src = fields_move(t, k)
                        move_bank(step, dst, src)
                elif kind == "gram":
                    if wide_no(step) == 0:
                        dve.wait_ge(w_in, 16 * 6)
                    for s in range(4):
                        dve.wait_ge(base_copied, 4 * wide_no(step) + s + 1)
                        for x in range(4):
                            dst, src = merged(t, k, s, x, 0)
                            part = own[SLOTS * x:SLOTS * (x + 1), 0:KX[x]]
                            last = nc.vector.copy_predicated(dst, part[:, :, None].to_broadcast(dst.shape), src)
                    last.then_inc(wide_moved, 1)
                elif kind == "layer1":
                    dve.wait_ge(h1_full, 2 * t + 2)
                    for o in range(2):
                        last = nc.vector.tensor_scalar(h1[:, 2 + o, :], acc[1][:, o, :], b1_sb[:, 2 + o:3 + o], 0.0,
                                                       ALU.add, ALU.max)
                    last.then_inc(h1_moved[1], 1)
                elif kind == "layer2":
                    dve.wait_ge(h2_full, 2 * t + 2)
                    nc.vector.tensor_scalar(h2[:, 1, :], acc[1][:, 2, :], b2_sb[:, 1:2], 0.0, ALU.add,
                                            ALU.max).then_inc(h2_moved[1], 1)
                elif kind == "layer3":
                    dve.wait_ge(y_full, t + 1)
                    nc.vector.tensor_copy(y[:, t * P:(t + 1) * P].rearrange("o (j s) -> o s j", s=4),
                                          acc[0][0:1, 3, :].rearrange("o (s j) -> o s j", s=4)).then_inc(y_moved, 1)

        @block.tensor
        def _(pe):
            def bank_turn(step):
                n = bank_no(step)
                if n >= 2:
                    wait_bank_moved(pe, n - 2)
                return n % 2

            for kind, t, k in steps:
                step = (kind, t, k)
                if kind == "dense":
                    pe.wait_ge(ident_ready, 1)
                    pe.wait_ge(dense_in, 16)
                    n = bank_turn(step)
                    for i in range(TILES):
                        last = nc.tensor.transpose(bank[:, n, i * P:(i + 1) * P], dense_sb[:, i, :], ident[:, :])
                    last.then_inc(bank_full, 1)
                elif kind == "match":
                    n = bank_turn(step)
                    pe.wait_ge(lo_ready, t + 1)
                    for r in range(ROWS):
                        pe.wait_ge(mask_ready, t * ROWS + r + 1)
                        m = mask[(t * ROWS + r) % MASKS][:, :]
                        nc.tensor.matmul(bank[:, n, :], hi[t % 2][:, r * D:(r + 1) * D], m,
                                         start=(r == 0), stop=False)
                        last = nc.tensor.matmul(bank[:, n, :], lo[t % 2][:, r * D:(r + 1) * D], m,
                                                start=False, stop=(r == ROWS - 1))
                        last.then_inc(mask_used, 1)
                elif kind == "fields":
                    pe.wait_ge(rows_in[t][k], 16 * len(GROUPS[k]))
                    n = bank_turn(step)
                    for i, g in enumerate(GROUPS[k]):
                        last = nc.tensor.transpose(bank[:, n, i * P:(i + 1) * P], rows[:, t, g, :], ident[:, :])
                    last.then_inc(bank_full, 1)
                elif kind == "gram":
                    if k == 0:
                        u = bank_no(("fields", t, len(GROUPS) - 1))
                        wait_bank_moved(pe, u)
                        wait_bank_moved(pe, u - 1)
                    n = wide_no(step)
                    j0, j1 = BATCHES[t][k]
                    before = [m for m, (_, u, v) in enumerate(wide_steps[:n])
                              if BATCHES[u][v][0] % 16 < j0 % 16 + j1 - j0 and
                              j0 % 16 < BATCHES[u][v][0] % 16 + BATCHES[u][v][1] - BATCHES[u][v][0]]
                    if before:
                        pe.wait_ge(wide_moved, before[-1] + 1)
                    else:
                        pe.wait_ge(spare_ready, 2)
                    for j in range(j0, j1):
                        b = t * P + 4 * j
                        last = nc.tensor.matmul(wide[:, j % 16, 0:4 * NV],
                                                embT[:, b:b + 4, :].rearrange("p s a -> p (s a)"),
                                                embT[:, b:b + 4, 0:NV], start=True, stop=True)
                    last.then_inc(wide_full, 1)
                elif kind == "layer1":
                    pe.wait_ge(wide_moved, wide_no(("gram", t, len(BATCHES[t]) - 1)) + 1)
                    if t == 0:
                        pe.wait_ge(w_in, 16 * 6)
                        pe.wait_ge(w1d_ready, 1)
                    else:
                        pe.wait_ge(y_moved, t)
                    x = denseT[:, t, :, :].rearrange("p s j -> p (s j)")
                    for o in range(H1 // P):
                        cols = slice(o * P, (o + 1) * P)
                        dst = acc[o // 2][:, o % 2, :]
                        nc.tensor.matmul(dst, w1d[:, cols], x, start=True, stop=False)
                        for g in range(KC):
                            last = nc.tensor.matmul(dst, w1_sb[0:KROWS[g], g, cols],
                                                    pairsT[t % 2][0:KROWS[g], g, :, :].rearrange("p s j -> p (s j)"),
                                                    start=False, stop=(g == KC - 1))
                        if o % 2:
                            last.then_inc(h1_full, 1)
                elif kind == "layer2":
                    for o, i in [(0, 0), (0, 1), (0, 2), (0, 3), (1, 0), (1, 1), (1, 2), (1, 3)]:
                        if o == 0 and i % 2 == 0:
                            pe.wait_ge(h1_moved[i // 2], t + 1)
                        last = nc.tensor.matmul(acc[o][:, 2, :], w2_sb[:, i, o * P:(o + 1) * P], h1[:, i, :],
                                                start=(i == 0), stop=(i == H1 // P - 1))
                        if i == H1 // P - 1:
                            last.then_inc(h2_full, 1)
                elif kind == "layer3":
                    for i in range(H2 // P):
                        pe.wait_ge(h2_moved[i], t + 1)
                    for i in range(H2 // P):
                        last = nc.tensor.matmul(acc[0][0:1, 3, :], w3_sb[:, i:i + 1], h2[:, i, :],
                                                start=(i == 0), stop=(i == H2 // P - 1))
                    last.then_inc(y_full, 1)


def kernel(**inputs):
    import numpy as np
    import concourse.bacc as bacc
    from concourse import mybir
    from concourse.bass_utils import run_bass_kernel_spmd as run

    nc = bacc.Bacc("TRN2", target_bir_lowering=False, num_devices=1)
    data = {name: np.ascontiguousarray(a) for name, a in inputs.items()}
    data["ids_row"] = np.ascontiguousarray(data["ids"].T[MATCHED])
    w1p = np.zeros((P, KC, H1), data["W_top1"].dtype)
    chunk, part, row = (list(x) for x in zip(*pair_rows()))
    w1p[part, chunk] = data["W_top1"][row]
    data["own_rows"] = np.array([[serves_itself(4 * g + p // SLOTS, p % SLOTS) for g in range(KC)]
                                 for p in range(P)], np.int32)
    data["w1p"] = w1p.reshape(P, KC * H1)
    arrays, h = {}, {}
    for name, a in data.items():
        arrays[name + "_in"] = a
        h[name] = nc.dram_tensor(name + "_in", a.shape, mybir.dt.from_np(a.dtype), kind="ExternalInput").ap()
    out = nc.dram_tensor("y_out", (B, 1), mybir.dt.float32, kind="ExternalOutput").ap()
    program(nc, h["r_dense_features"], h["ids"], h["ids_row"], [h[f"tbl_{f}"] for f in range(F)], h["w1p"],
            h["W_top1"], h["own_rows"], h["b_top1"], h["W_top2"], h["b_top2"], h["W_top3"], out)
    r = run(nc, [arrays], core_ids=[0])
    return r.results[0]["y_out"]
```

```python
import concourse.bass as bass
from concourse import mybir
from contextlib import ExitStack

B, F, D = 512, 26, 128
P = 128
TILES = B // P
H1, H2 = 512, 256
VOCAB = 1000
MATCHED = [0, 4, 7, 8, 16, 18, 19, 22]
GATHERED = [f for f in range(F) if f not in MATCHED]
NM, NG = len(MATCHED), len(GATHERED)
NV = F + 1
SLOT_VECTORS = [0] + [1 + f for f in MATCHED] + [1 + f for f in GATHERED]
G0 = 1 + NM
SLOTS = 32
ROWS = 8
TP = VOCAB // ROWS
RAWS = 3
DVE_MASKS = ROWS - 1
HALF = NV // 2
MERGED = HALF + 1
KC = -(-MERGED // 4)
KX = [len(range(x, MERGED, 4)) for x in range(4)]
KROWS = [SLOTS * min(4, MERGED - 4 * g) for g in range(KC)]
GROUPS = [list(range(NG))[i:i + 4] for i in range(0, NG, 4)]
NJ = P // 4
PLACES = 16
BATCH = PLACES // 2
BATCHES = NJ // BATCH
FILLS = PLACES + 6


def serves_itself(k, a):
    return 1 <= a - k <= HALF


def pair_rows():
    out = []
    for k in range(MERGED):
        for a in range(NV):
            c = k if serves_itself(k, a) else k + HALF + 1
            if c < NV and c != a:
                u, v = sorted((SLOT_VECTORS[c], SLOT_VECTORS[a]))
                row = D + v - 1 if u == 0 else D + F + (u - 1) * F - u * (u - 1) // 2 + v - u - 1
                out.append((k // 4, SLOTS * (k % 4) + a, row))
    assert len({row for _, _, row in out}) == len(out) == NV * (NV - 1) // 2
    return out


def program(nc, dense, ids, ids_row, tables, w1p, w1, own_rows, b1, w2, b2, w3, out):
    fp32, f32r, i32 = mybir.dt.float32, mybir.dt.float32r, mybir.dt.int32
    ALU, ACT = mybir.AluOpType, mybir.ActivationFunctionType
    ctx = ExitStack()
    with ctx:
        def sb(name, shape, dt=fp32):
            return ctx.enter_context(nc.sbuf_tensor(name, shape, dt))

        def ps(name, shape):
            return ctx.enter_context(nc.psum_tensor(name, shape, fp32))

        def sem(name):
            return ctx.enter_context(nc.semaphore(name))

        ident = sb("ident", [P, P])
        row_no = sb("row_no", [TP, ROWS])
        minus_row = sb("minus_row", [TP, ROWS])
        distance = sb("distance", [TP, B])
        idx = sb("idx", [P, TILES, F], i32)
        idsb = sb("idsb", [P, NM, B], i32)
        raw = sb("raw", [TP, RAWS, ROWS * D])
        hi = [sb(f"hi{i}", [TP, ROWS * D], f32r) for i in range(2)]
        lo = [sb(f"lo{i}", [TP, ROWS * D], f32r) for i in range(2)]
        mask = [sb(f"mask{i}", [TP, B], f32r) for i in range(ROWS)]
        rows = sb("rows", [P, TILES, NG, D])
        dense_sb = sb("dense_sb", [P, TILES, D])
        embT = sb("embT", [P, B, SLOTS])
        denseT = sb("denseT", [P, TILES, 4, P // 4])
        own = sb("own", [P, KC], i32)
        pairsT = [sb(f"pairsT{i}", [P, KC, 4, NJ]) for i in range(2)]
        w1_sb = sb("w1_sb", [P, KC, H1])
        w1a = sb("w1a", [P, H1])
        w1b = sb("w1b", [P, H1])
        w1d = sb("w1d", [P, H1])
        w2_sb = sb("w2_sb", [P, H1 // P, H2])
        w3_sb = sb("w3_sb", [P, H2 // P])
        b1_sb = sb("b1_sb", [P, H1 // P])
        b2_sb = sb("b2_sb", [P, H2 // P])
        h1 = sb("h1", [P, H1 // P, P])
        h2 = sb("h2", [P, H2 // P, P])
        y = sb("y", [1, B])

        bank = ps("bank", [P, 2, 512])
        wide = ps("wide", [P, PLACES, P])
        acc = [ps(f"acc{i}", [P, 4, P]) for i in range(2)]

        ids_in = sem("ids_in")
        idsb_in = [sem(f"idsb_in{m}") for m in range(NM)]
        raw_in = [sem(f"raw_in{i}") for i in range(RAWS)]
        dense_in = sem("dense_in")
        w1_in = sem("w1_in")
        w_in = sem("w_in")
        rows_in = [[sem(f"rows_in{t}_{g}") for g in range(len(GROUPS))] for t in range(TILES)]
        ident_zero = sem("ident_zero")
        ident_ready = sem("ident_ready")
        row_no_ready = sem("row_no_ready")
        spare_ready = sem("spare_ready")
        w1d_ready = sem("w1d_ready")
        hi_ready = sem("hi_ready")
        lo_ready = sem("lo_ready")
        mask_ready = sem("mask_ready")
        minus_row_ready = sem("minus_row_ready")
        act_mask_ready = sem("act_mask_ready")
        distance_ready = sem("distance_ready")
        mask_used = sem("mask_used")
        bank_full = sem("bank_full")
        bank_moved = [sem("bank_moved0"), sem("bank_moved1")]
        match_moved = sem("match_moved")
        wide_full = sem("wide_full")
        base_copied = sem("base_copied")
        wide_moved = sem("wide_moved")
        h1_full = sem("h1_full")
        h1_moved = [sem("h1_moved0"), sem("h1_moved1")]
        out_done = sem("out_done")

        early = [("fields", t, g) for t in range(2) for g in range(len(GROUPS))]
        steps = []
        for m in range(NM):
            take = 0 if m < 2 else 1
            steps += [("match", m, 0)] + ([("dense", 0, 0)] if m == 1 else []) + early[:take]
            early = early[take:]
        assert early[0] == ("fields", 1, 1)
        steps += [
            ("fields", 1, 1), ("gram", 0, 0), ("gram", 0, 1), ("fields", 1, 2), ("layer1 dense", 0, 0),
            ("layer1 dense", 0, 1), ("gram", 0, 2), ("fields", 1, 3), ("fields", 1, 4), ("gram", 0, 3),
            ("gram", 1, 0), ("fields", 2, 0), ("gram", 1, 1), ("layer1", 0, 0), ("layer1", 0, 1), ("fields", 2, 1),
            ("gram", 1, 2), ("fields", 2, 2), ("gram", 1, 3), ("fields", 2, 3), ("layer2", 0, 0), ("layer2", 0, 1),
            ("fields", 2, 4), ("layer1 dense", 1, 0), ("layer1 dense", 1, 1), ("layer3", 0, 0), ("gram", 2, 0),
            ("gram", 2, 1), ("fields", 3, 0), ("layer1", 1, 0), ("layer1", 1, 1), ("fields", 3, 1), ("gram", 2, 2),
            ("layer1 dense", 2, 0), ("layer1 dense", 2, 1), ("fields", 3, 2), ("gram", 2, 3), ("layer2", 1, 0),
            ("layer2", 1, 1), ("fields", 3, 3), ("layer1", 2, 0), ("fields", 3, 4), ("layer1", 2, 1),
            ("gram", 3, 0), ("gram", 3, 1), ("layer3", 1, 0), ("layer1 dense", 3, 0), ("gram", 3, 2),
            ("gram", 3, 3), ("layer1 dense", 3, 1), ("layer2", 2, 0), ("layer2", 2, 1), ("layer1", 3, 0),
            ("layer1", 3, 1), ("layer3", 2, 0), ("layer2", 3, 0), ("layer2", 3, 1), ("layer3", 3, 0)]
        BANK = ("dense", "fields", "layer2", "layer3")
        bank_steps = [s for s in steps if s[0] in BANK]
        wide_steps = [s for s in steps if s[0] == "gram"]

        def bank_no(step):
            return bank_steps.index(step)

        def wide_no(step):
            return wide_steps.index(step)

        def wait_bank_moved(eng, n):
            eng.wait_ge(bank_moved[n % 2], n // 2 + 1)

        def wait_bank_full(eng, step):
            eng.wait_ge(bank_full, bank_no(step) + 1)

        def fields_move(t, g):
            group = GROUPS[g]
            n = bank_no(("fields", t, g)) % 2
            dst = embT[:, t * P:(t + 1) * P, G0 + group[0]:G0 + group[0] + len(group)].rearrange("p b f -> p f b")
            return dst, bank[:, n, 0:len(group) * P].rearrange("p (f b) -> p f b", b=P)

        def merged(t, n, s, x, first):
            j = n * BATCH
            at = j % PLACES
            dst = pairsT[t % 2][SLOTS * x:SLOTS * (x + 1), 0:KX[x], s, j:j + BATCH]
            c = NV * s + first + x
            src = wide[SLOTS * s:SLOTS * (s + 1), at:at + BATCH, c:c + 4 * KX[x] - 3:4].rearrange("p j g -> p g j")
            return dst, src

        def moved_by_act(t, g):
            return t < 3 or bank_no(("fields", t, g)) % 2 == 0

        block = ctx.enter_context(nc.Block())

        @block.sync
        def _(sp):
            sp.dma_start(idx[:, :, :], ids.rearrange("(t p) f -> p t f", p=P)).then_inc(ids_in, 16)
            for m, f in enumerate(MATCHED):
                sp.dma_start(idsb[:, m, :], ids_row[m:m + 1, :].to_broadcast([P, B])).then_inc(idsb_in[m], 16)
                if m >= RAWS:
                    sp.wait_ge(hi_ready, m - RAWS + 1)
                    sp.wait_ge(lo_ready, m - RAWS + 1)
                table = tables[f].rearrange("(p r) d -> p (r d)", r=ROWS)
                full = TP // 16 * 16
                sp.dma_start(raw[0:full, m % RAWS, :], table[0:full, :]).then_inc(raw_in[m % RAWS], 16)
                sp.dma_start(raw[full:TP, m % RAWS, :], table[full:TP, :]).then_inc(raw_in[m % RAWS], 16)
                if m == 1:
                    sp.dma_start(dense_sb[:, :, :], dense.rearrange("(t p) d -> p t d", p=P)).then_inc(dense_in, 16)
            sp.dma_start(w1_sb[:, :, :], w1p.rearrange("p (k n) -> p k n", k=KC)).then_inc(w_in, 16)
            sp.dma_start(w1a[:, :], w1[0:D, :]).then_inc(w1_in, 16)
            sp.dma_start(w1b[:, :], w1[D + F + F * (F - 1) // 2:, :]).then_inc(w1_in, 16)
            sp.dma_start(w2_sb[:, :, :], w2.rearrange("(k p) n -> p k n", p=P)).then_inc(w_in, 16)
            with nc.allow_non_contiguous_dma(reason="small vectors laid on partitions"):
                sp.dma_start(own[:, :], own_rows).then_inc(w_in, 16)
                sp.dma_start(w3_sb[:, :], w3.rearrange("(k p) o -> p (k o)", p=P)).then_inc(w_in, 16)
                sp.dma_start(b1_sb[:, :], b1.rearrange("(k p) -> p k", p=P)).then_inc(w_in, 16)
                sp.dma_start(b2_sb[:, :], b2.rearrange("(k p) -> p k", p=P)).then_inc(w_in, 16)
            for i in range(2):
                sp.wait_ge(bank_moved[i], len(range(i, len(bank_steps), 2)))
            sp.dma_start(out.rearrange("b o -> o b"), y[:, :]).then_inc(out_done, 16)
            sp.wait_ge(out_done, 16)

        @block.gpsimd
        def _(pool):
            nc.gpsimd.iota(row_no[:, :], pattern=[[1, ROWS]], base=0, channel_multiplier=ROWS,
                           allow_small_or_imprecise_dtypes=True).then_inc(row_no_ready, 1)
            nc.gpsimd.memset(ident[:, :], 0.0).then_inc(ident_zero, 1)
            pool.wait_ge(ident_zero, 1)
            nc.gpsimd.affine_select(out=ident[:, :], in_=ident[:, :], compare_op=ALU.not_equal, fill=1.0, base=0,
                                    pattern=[[-1, P]], channel_multiplier=1).then_inc(ident_ready, 1)
            pool.wait_ge(ids_in, 16)
            for t in range(TILES):
                for g, group in enumerate(GROUPS):
                    for n in group:
                        f = GATHERED[n]
                        pool.indirect_dma_start(
                            out=rows[:, t, n, :], out_offset=None, in_=tables[f],
                            in_offset=bass.IndirectOffsetOnAxis(ap=idx[:, t, f:f + 1], axis=0),
                        ).then_inc(rows_in[t][g], 16)

        @block.scalar
        def _(act):
            def split(m):
                act.wait_ge(raw_in[m % RAWS], 32 * (m // RAWS + 1))
                if m >= 2:
                    act.wait_ge(mask_used, ROWS * (m - 1))
                nc.scalar.activation(hi[m % 2][:, :], raw[:, m % RAWS, :], ACT.Copy).then_inc(hi_ready, 1)

            def move_bank(step, dst, src):
                n = bank_no(step)
                wait_bank_full(act, step)
                nc.scalar.activation(dst, src, ACT.Copy).then_inc(bank_moved[n % 2], 1)

            def distances(m):
                act.wait_ge(idsb_in[m], 16)
                if m:
                    act.wait_ge(act_mask_ready, m)
                nc.scalar.activation(distance[:, :], idsb[0:TP, m, :], ACT.Abs,
                                     bias=minus_row[:, ROWS - 1:ROWS]).then_inc(distance_ready, 1)

            def last_mask(m):
                act.wait_ge(distance_ready, m + 1)
                nc.scalar.activation(mask[ROWS - 1][:, :], distance[:, :], ACT.Relu, scale=-1.0,
                                     bias=1.0).then_inc(act_mask_ready, 1)

            act.wait_ge(row_no_ready, 1)
            nc.scalar.activation(minus_row[:, :], row_no[:, :], ACT.Copy, scale=-1.0).then_inc(minus_row_ready, 1)
            act.wait_ge(minus_row_ready, 1)
            split(0)
            distances(0)
            last_mask(0)
            split(1)
            for kind, t, k in steps:
                step = (kind, t, k)
                if kind == "dense":
                    src = bank[:, bank_no(step) % 2, :]
                    wait_bank_full(act, step)
                    nc.scalar.activation(denseT[:, :, :, :], src.rearrange("p (t j s) -> p t s j", s=4, t=TILES),
                                         ACT.Copy)
                    move_bank(step, embT[:, :, 0], src)
                elif kind == "match":
                    if t + 1 < NM:
                        distances(t + 1)
                    act.wait_ge(mask_used, ROWS * (t + 1))
                    if t + 1 < NM:
                        last_mask(t + 1)
                    if t + 2 < NM:
                        split(t + 2)
                    nc.scalar.activation(embT[:, :, 1 + t], acc[t % 2][:, :, :].rearrange("p o b -> p (o b)"),
                                         ACT.Copy).then_inc(match_moved, 1)
                elif kind == "fields" and moved_by_act(t, k):
                    dst, src = fields_move(t, k)
                    move_bank(step, dst, src)
                elif kind == "gram":
                    act.wait_ge(wide_full, wide_no(step) + 1)
                    for s in range(4):
                        for x in range(4):
                            dst, src = merged(t, k, s, x, HALF + 1)
                            last = nc.scalar.activation(dst, src, ACT.Copy)
                        last.then_inc(base_copied, 1)
                elif kind == "layer1" and k == 0:
                    act.wait_ge(h1_full, 2 * t + 1)
                    if t == 0:
                        act.wait_ge(w_in, 16 * 6)
                    for o in range(2):
                        last = nc.scalar.activation(h1[:, o, :], acc[0][:, o, :], ACT.Relu, bias=b1_sb[:, o:o + 1])
                    last.then_inc(h1_moved[0], 1)
                elif kind == "layer2" and k == 0:
                    n = bank_no(step)
                    wait_bank_full(act, step)
                    nc.scalar.activation(h2[:, 0, :], bank[:, n % 2, 0:P], ACT.Relu,
                                         bias=b2_sb[:, 0:1]).then_inc(bank_moved[n % 2], 1)

        @block.vector
        def _(dve):
            def masks(m, chunks=range(DVE_MASKS)):
                dve.wait_ge(idsb_in[m], 16)
                for r in chunks:
                    if m:
                        dve.wait_ge(mask_used, (m - 1) * ROWS + r + 1)
                    nc.vector.tensor_scalar(mask[r][:, :], idsb[0:TP, m, :], row_no[:, r:r + 1], None,
                                            ALU.is_equal).then_inc(mask_ready, 1)

            def split(m):
                dve.wait_ge(hi_ready, m + 1)
                if m >= 2:
                    dve.wait_ge(mask_used, ROWS * (m - 1))
                nc.vector.tensor_tensor(lo[m % 2][:, :], raw[:, m % RAWS, :], hi[m % 2][:, :].bitcast(fp32),
                                        ALU.subtract).then_inc(lo_ready, 1)

            def move_bank(step, dst, src):
                n = bank_no(step)
                wait_bank_full(dve, step)
                nc.vector.tensor_copy(dst, src).then_inc(bank_moved[n % 2], 1)

            nc.vector.memset(embT[:, :, NV:SLOTS], 0.0).then_inc(spare_ready, 1)
            dve.wait_ge(row_no_ready, 1)
            for kind, t, k in steps:
                step = (kind, t, k)
                if kind == "match":
                    if t == 0:
                        masks(0)
                        split(0)
                    if t + 1 < NM:
                        early_masks = 0 if t <= 2 else 3
                        masks(t + 1, range(0, early_masks))
                        split(t + 1)
                        masks(t + 1, range(early_masks, DVE_MASKS))
                elif kind == "fields":
                    if t == 1 and k == 0:
                        dve.wait_ge(w1_in, 32)
                        nc.vector.tensor_tensor(w1d[:, :], w1a[:, :], w1b[:, :], ALU.add).then_inc(w1d_ready, 1)
                    if not moved_by_act(t, k):
                        dst, src = fields_move(t, k)
                        move_bank(step, dst, src)
                elif kind == "gram":
                    if wide_no(step) == 0:
                        dve.wait_ge(w_in, 16 * 6)
                    for s in range(4):
                        dve.wait_ge(base_copied, 4 * wide_no(step) + s + 1)
                        for x in range(4):
                            dst, src = merged(t, k, s, x, 0)
                            part = own[SLOTS * x:SLOTS * (x + 1), 0:KX[x]]
                            last = nc.vector.copy_predicated(dst, part[:, :, None].to_broadcast(dst.shape), src)
                    last.then_inc(wide_moved, 1)
                elif kind == "layer1" and k == 1:
                    dve.wait_ge(h1_full, 2 * t + 2)
                    for o in range(2):
                        last = nc.vector.tensor_scalar(h1[:, 2 + o, :], acc[1][:, o, :], b1_sb[:, 2 + o:3 + o], 0.0,
                                                       ALU.add, ALU.max)
                    last.then_inc(h1_moved[1], 1)
                elif kind == "layer2" and k == 1:
                    n = bank_no(step)
                    wait_bank_full(dve, step)
                    nc.vector.tensor_scalar(h2[:, 1, :], bank[:, n % 2, 0:P], b2_sb[:, 1:2], 0.0, ALU.add,
                                            ALU.max).then_inc(bank_moved[n % 2], 1)
                elif kind == "layer3":
                    move_bank(step, y[:, t * P:(t + 1) * P].rearrange("o (j s) -> o s j", s=4),
                              bank[0:1, bank_no(step) % 2, 0:P].rearrange("o (s j) -> o s j", s=4))

        @block.tensor
        def _(pe):
            def bank_turn(step):
                n = bank_no(step)
                if n >= 2:
                    wait_bank_moved(pe, n - 2)
                return n % 2

            pe.wait_ge(ident_ready, 1)
            for j in range(FILLS):
                nc.tensor.transpose(wide[:, j % PLACES, :], ident[:, :], ident[:, :])
            for kind, t, k in steps:
                step = (kind, t, k)
                if kind == "dense":
                    pe.wait_ge(dense_in, 16)
                    n = bank_turn(step)
                    for i in range(TILES):
                        last = nc.tensor.transpose(bank[:, n, i * P:(i + 1) * P], dense_sb[:, i, :], ident[:, :])
                    last.then_inc(bank_full, 1)
                elif kind == "match":
                    if t >= 2:
                        pe.wait_ge(match_moved, t - 1)
                    dst = acc[t % 2][:, :, :].rearrange("p o b -> p (o b)")
                    pe.wait_ge(hi_ready, t + 1)
                    order = [(r, part) for r in range(ROWS) for part in (hi, lo)]
                    if t == 0:
                        order.sort(key=lambda x: x[1] is lo)
                    for n, (r, part) in enumerate(order):
                        if part is lo:
                            pe.wait_ge(lo_ready, t + 1)
                        elif r < DVE_MASKS:
                            pe.wait_ge(mask_ready, t * DVE_MASKS + r + 1)
                        else:
                            pe.wait_ge(act_mask_ready, t + 1)
                        last = nc.tensor.matmul(dst, part[t % 2][:, r * D:(r + 1) * D], mask[r][:, :],
                                                start=(n == 0), stop=(n == len(order) - 1))
                        if part is lo:
                            last.then_inc(mask_used, 1)
                elif kind == "fields":
                    pe.wait_ge(rows_in[t][k], 16 * len(GROUPS[k]))
                    n = bank_turn(step)
                    for i, g in enumerate(GROUPS[k]):
                        last = nc.tensor.transpose(bank[:, n, i * P:(i + 1) * P], rows[:, t, g, :], ident[:, :])
                    last.then_inc(bank_full, 1)
                elif kind == "gram":
                    if k == 0:
                        u = bank_no(("fields", t, len(GROUPS) - 1))
                        wait_bank_moved(pe, u)
                        wait_bank_moved(pe, u - 1)
                        if t == 0:
                            pe.wait_ge(match_moved, NM)
                    n = wide_no(step)
                    if n >= 2:
                        pe.wait_ge(wide_moved, n - 1)
                    else:
                        pe.wait_ge(spare_ready, 1)
                    for j in range(k * BATCH, (k + 1) * BATCH):
                        b = t * P + 4 * j
                        last = nc.tensor.matmul(wide[:, j % PLACES, 0:4 * NV],
                                                embT[:, b:b + 4, :].rearrange("p s a -> p (s a)"),
                                                embT[:, b:b + 4, 0:NV], start=True, stop=True)
                    last.then_inc(wide_full, 1)
                elif kind == "layer1 dense":
                    if t == 0:
                        pe.wait_ge(w1d_ready, 1)
                        pe.wait_ge(match_moved, NM)
                    else:
                        pe.wait_ge(h1_moved[k], t)
                    for o in (2 * k, 2 * k + 1):
                        nc.tensor.matmul(acc[k][:, o % 2, :], w1d[:, o * P:(o + 1) * P],
                                         denseT[:, t, :, :].rearrange("p s j -> p (s j)"),
                                         start=(o % 2 == 0), stop=False)
                elif kind == "layer1":
                    if t == 0:
                        pe.wait_ge(w_in, 16 * 6)
                    pe.wait_ge(wide_moved, wide_no(("gram", t, BATCHES - 1)) + 1)
                    for o in (2 * k, 2 * k + 1):
                        for g in range(KC):
                            last = nc.tensor.matmul(acc[k][:, o % 2, :],
                                                    w1_sb[0:KROWS[g], g, o * P:(o + 1) * P],
                                                    pairsT[t % 2][0:KROWS[g], g, :, :].rearrange("p s j -> p (s j)"),
                                                    start=False, stop=(o % 2 == 1 and g == KC - 1))
                    last.then_inc(h1_full, 1)
                elif kind == "layer2":
                    n = bank_turn(step)
                    for i in range(H1 // P):
                        if i % 2 == 0:
                            pe.wait_ge(h1_moved[i // 2], t + 1)
                        last = nc.tensor.matmul(bank[:, n, 0:P], w2_sb[:, i, k * P:(k + 1) * P], h1[:, i, :],
                                                start=(i == 0), stop=(i == H1 // P - 1))
                    last.then_inc(bank_full, 1)
                elif kind == "layer3":
                    for i in range(H2 // P):
                        wait_bank_moved(pe, bank_no(("layer2", t, i)))
                    n = bank_turn(step)
                    for i in range(H2 // P):
                        last = nc.tensor.matmul(bank[0:1, n, 0:P], w3_sb[:, i:i + 1], h2[:, i, :],
                                                start=(i == 0), stop=(i == H2 // P - 1))
                    last.then_inc(bank_full, 1)


def kernel(**inputs):
    import numpy as np
    import concourse.bacc as bacc
    from concourse import mybir
    from concourse.bass_utils import run_bass_kernel_spmd as run

    nc = bacc.Bacc("TRN2", target_bir_lowering=False, num_devices=1)
    data = {name: np.ascontiguousarray(a) for name, a in inputs.items()}
    data["ids_row"] = np.ascontiguousarray(data["ids"].T[MATCHED])
    w1p = np.zeros((P, KC, H1), data["W_top1"].dtype)
    chunk, part, row = (list(x) for x in zip(*pair_rows()))
    w1p[part, chunk] = data["W_top1"][row]
    data["own_rows"] = np.array([[serves_itself(4 * g + p // SLOTS, p % SLOTS) for g in range(KC)]
                                 for p in range(P)], np.int32)
    data["w1p"] = w1p.reshape(P, KC * H1)
    arrays, h = {}, {}
    for name, a in data.items():
        arrays[name + "_in"] = a
        h[name] = nc.dram_tensor(name + "_in", a.shape, mybir.dt.from_np(a.dtype), kind="ExternalInput").ap()
    out = nc.dram_tensor("y_out", (B, 1), mybir.dt.float32, kind="ExternalOutput").ap()
    program(nc, h["r_dense_features"], h["ids"], h["ids_row"], [h[f"tbl_{f}"] for f in range(F)], h["w1p"],
            h["W_top1"], h["own_rows"], h["b_top1"], h["W_top2"], h["b_top2"], h["W_top3"], out)
    r = run(nc, [arrays], core_ids=[0])
    return r.results[0]["y_out"]
```
